# Optimizing a Trainium2 kernel written in Bass

```python
import numpy as np
import jax
import jax.numpy as jnp

def _softmax(x, axis=-1):
    return jax.nn.softmax(x, axis=axis)

def _gelu(x):
    return jax.nn.gelu(x, approximate=True)

def _silu(x):
    return jax.nn.silu(x)

def _sigmoid(x):
    return jax.nn.sigmoid(x)

def _layernorm(x, axis=-1, eps=1e-05):
    m = jnp.mean(x, axis=axis, keepdims=True)
    v = jnp.var(x, axis=axis, keepdims=True)
    return (x - m) / jnp.sqrt(v + eps)

def _scatter_add(tgt, idx, src, axis=0):
    return tgt.at[idx].add(src)

def _segment_sum(src, seg, n):
    return jax.ops.segment_sum(src, seg, n)
kernel_name = 'mk_adj_resnorm_d2_adj_r2_21e644'

def setup_inputs(seed: int=0):
    np.random.seed(seed)
    _w = jnp.asarray

    def _rec_inputs():
        import jax
        import jax.numpy as jnp
        _gk = jax.random.key(seed)
        x = -0.0002928 + 1 * jax.random.normal(jax.random.fold_in(_gk, 1), (4096, 256), jnp.float32)
        _a = jax.random.bernoulli(jax.random.fold_in(_gk, 2), 0.00195312, (4096, 4096))
        _a = jnp.logical_or(_a, jnp.eye(4096, dtype=bool))
        _af = _a.astype(jnp.float32)
        _af = _af * jax.random.uniform(jax.random.fold_in(_gk, 3), (4096, 4096), jnp.float32, 0.05, 1)
        adj = _af
        return (x, adj)
    x, adj = _rec_inputs()

    def _L0_gnn_setup():
        import jax, jax.numpy as jnp
        import numpy as np
        N = 4096
        IN_C = 256
        OUT_C = 256
        key = jax.random.key(seed)
        k1, k2, k3 = jax.random.split(key, 3)
        x = jax.random.normal(k1, (N, IN_C), dtype=jnp.float32)
        adj = jax.random.uniform(k2, (N, N), dtype=jnp.float32)
        w = jax.random.uniform(k3, (IN_C, OUT_C), dtype=jnp.float32)
        return {'x': x, 'adj': adj, 'w': w}
    _L0_gnn_all = _L0_gnn_setup()
    _L0_gnn_in = {k: v for k, v in _L0_gnn_all.items() if k in ('w',)}
    del _L0_gnn_all

    def _L1_gnn_setup():
        import jax, jax.numpy as jnp
        import numpy as np
        N_NODES = 4096
        DIM = 256
        key = jax.random.key(seed)
        k1, k2, k3, k4 = jax.random.split(key, 4)
        x = jax.random.normal(k1, (N_NODES, DIM), dtype=jnp.float32)
        adj = jax.random.uniform(k2, (N_NODES, N_NODES), dtype=jnp.float32)
        bound = 1.0 / np.sqrt(DIM)
        W = jax.random.uniform(k3, (DIM, DIM), minval=-bound, maxval=bound, dtype=jnp.float32)
        b = jax.random.uniform(k4, (DIM,), minval=-bound, maxval=bound, dtype=jnp.float32)
        return {'x': x, 'adj': adj, 'W': W, 'b': b}
    _L1_gnn_all = _L1_gnn_setup()
    _L1_gnn_in = {k: v for k, v in _L1_gnn_all.items() if k in ('W', 'b')}
    del _L1_gnn_all
    return {'x': x, 'adj': adj, 'L0_gnn_w': _L0_gnn_in['w'], 'L1_gnn_W': _L1_gnn_in['W'], 'L1_gnn_b': _L1_gnn_in['b']}

def reference(x, adj, L0_gnn_w, L1_gnn_W, L1_gnn_b):
    import jax
    import jax.numpy as jnp

    def _L0_gnn_ref(x, adj, w):
        import jax, jax.numpy as jnp
        import numpy as np
        N = 4096
        IN_C = 256
        OUT_C = 256
        A = adj + jnp.eye(adj.shape[0], dtype=adj.dtype)
        deg = jnp.sum(A, axis=1)
        d_inv_sqrt = jax.lax.rsqrt(deg)
        A_hat = A * d_inv_sqrt[:, None] * d_inv_sqrt[None, :]
        mm_1 = A_hat @ x
        return jax.nn.elu(mm_1 @ w)

    def _L1_gnn_ref(x, adj, W, b):
        import jax, jax.numpy as jnp
        import numpy as np
        N_NODES = 4096
        DIM = 256
        agg = jnp.matmul(adj, x)
        out = jnp.matmul(agg, W.T) + b
        return jax.nn.relu(out)
    x = _layernorm(x + _L0_gnn_ref(x, adj, L0_gnn_w), axis=-1)
    x = _layernorm(x + _L1_gnn_ref(x, adj, L1_gnn_W, L1_gnn_b), axis=-1)
    return x

_drawn_inputs = setup_inputs


def setup_inputs(seed=0):
    import zlib

    import numpy as np

    out = dict(_drawn_inputs(seed))
    spreads = {}
    factors = {'L1_gnn_b': 3.03}
    for name, (base, spread) in spreads.items():
        noise = np.random.default_rng([zlib.crc32(name.encode()), seed]).standard_normal(out[name].shape)
        drawn = base * np.exp(spread * noise) if base else spread * noise
        out[name] = jnp.asarray(drawn.astype(out[name].dtype))
    for name, factor in factors.items():
        out[name] = (out[name] * factor).astype(out[name].dtype)
    return out
```

```python
from contextlib import ExitStack

import concourse.bass as bass
from concourse import mybir

P = 128
B32 = 32
F32 = mybir.dt.float32
F32R = mybir.dt.float32r
ALU = mybir.AluOpType
ACT = mybir.ActivationFunctionType
AX_X = mybir.AxisListType.X


def gnn_two_layers(nc: bass.Bass, x: bass.AP, adj: bass.AP, w: bass.AP, W: bass.AP, b: bass.AP, out: bass.AP):
    N, C = x.shape
    CH = C // P
    STRIPES = P // B32
    STRIPE = 256
    PANEL = STRIPES * STRIPE
    PANELS = N // PANEL
    TPP = STRIPE // B32
    GT = TPP // 2
    GN = GT * P
    GROUPS = 2 * PANELS
    RB = GN // B32
    EPS = 1e-5
    DEG_ON_DVE = GROUPS // 2
    JUNK = 4
    assert (CH, C) == (2, 256) and N == PANELS * PANEL

    def tiles(group):
        first = TPP * (group // 2) + group % 2
        return slice(first, first + 2 * GT - 1, 2)

    chunks = []
    units = []
    accs = []

    def add_chunk(name, row, panel, columns):
        chunks.append((name, row, panel, []))
        for col in columns:
            layer = 0 if name == "A" or (name == "B" and col >= row) else 1
            if not accs or accs[-1][:3] != (name, row, layer):
                accs.append((name, row, layer, len(units), None))
            accs[-1] = accs[-1][:4] + (len(units),)
            chunks[-1][3].append(len(units))
            units.append((name, row, col, len(chunks) - 1, len(accs) - 1))

    for row in range(GROUPS):
        for panel in range(PANELS):
            add_chunk("A", row, panel, [col for col in (2 * panel, 2 * panel + 1) if col < row])
    for row in range(GROUPS):
        own = row // 2
        for panel in ([*range(own + 1, PANELS), own, *range(own)] if row else range(PANELS)):
            both = (2 * panel, 2 * panel + 1)
            add_chunk("B", row, panel, both[::-1] if panel == own and row % 2 else both)
    for row in reversed(range(GROUPS)):
        for panel in range(row // 2, PANELS):
            add_chunk("C", row, panel, [col for col in (2 * panel, 2 * panel + 1) if col >= row])
    U = len(units)
    FIRST_B = next(n for n, c in enumerate(chunks) if c[0] == "B")
    rows_done = [a for a, s in enumerate(accs) if (s[0], s[2]) in (("B", 0), ("C", 1))]
    partials = [a for a in range(len(accs)) if a not in rows_done]
    order_of = {a: i for i, a in enumerate(rows_done)}
    partial_of = {a: i for i, a in enumerate(partials)}
    units_through = []
    for c in chunks:
        units_through.append((units_through[-1] if units_through else 0) + len(c[3]))

    AGG_AT, PROJECT_AT, ELU_AT, RESIDUAL_AT, NORM_AT = 2, 1, 3, 4, 6

    def ended(u, lag, which):
        return [a for a in which if accs[a][4] == u - lag]

    with ExitStack() as ctx:
        def sb(name, shape, dt=F32):
            return ctx.enter_context(nc.sbuf_tensor(name, shape, dt))

        def sem(name):
            return ctx.enter_context(nc.semaphore(name))

        v_hi = sb("v_hi", [P, N // P, C], F32R)
        v_lo = sb("v_lo", [P, N // P, C], F32R)
        partial = sb("partial", [P, GROUPS - 1, CH, GN])
        raw = [sb(f"raw{i}", [P, RB, STRIPE]) for i in range(2)]
        turned = [sb(f"turned{i}", [P, GT, GN]) for i in range(2)]
        a_hi = [sb(f"a_hi{i}", [P, GT, GN], F32R) for i in range(2)]
        a_lo = [sb(f"a_lo{i}", [P, GT, GN], F32R) for i in range(2)]
        agg = sb("agg", [P, CH, GN])
        x_row = sb("x_row", [P, GT, C])
        neg = sb("neg", [P, GT, C])
        res = sb("res", [P, GT, C])
        normed = sb("normed", [P, GT, C])
        w_sb = sb("w_sb", [P, CH, C])
        wt_sb = sb("wt_sb", [P, CH, C])
        b_sb = sb("b_sb", [P, C])
        ident = sb("ident", [P, P])
        fold = sb("fold", [P, B32])
        deg_parts = sb("deg_parts", [P, 2, PANELS, RB])
        deg_sums = sb("deg_sums", [P, RB])
        deg = sb("deg", [P, GT])
        dinv = sb("dinv", [P, N // P])
        ndinv = sb("ndinv", [P, N // P])
        stats = sb("stats", [P, GT, 6])
        mean_var = sb("mean_var", [P, GT, 2])
        rstd = sb("rstd", [P, GT])
        var_eps = sb("var_eps", [P, GT])
        minus_mean = sb("minus_mean", [P, GT])
        minus_half = sb("minus_half", [P, GT])
        shift = sb("shift", [P, GT])

        acc = [ctx.enter_context(nc.psum_tensor(f"acc{i}", [P, CH, GN], F32)) for i in range(3)]
        proj = ctx.enter_context(nc.psum_tensor("proj", [P, GT, C], F32))

        s_w = sem("weights_loaded")
        s_x = sem("x_loaded")
        s_raw = [sem(f"raw_loaded{i}") for i in range(2)]
        s_zero = sem("constants_zeroed")
        s_const = sem("constants_made")
        s_wt_mm = sem("wt_turned")
        s_wt = sem("wt_ready")
        s_degd = sem("deg_parts_dve")
        s_dega = sem("deg_parts_act")
        s_dsum = sem("deg_sums_ready")
        s_dmm = sem("deg_folded")
        s_deg = sem("deg_ready")
        s_pow = sem("dinv_made")
        s_dinv = sem("dinv_ready")
        s_yf = sem("y_scaled")
        s_vhi = sem("v_hi_ready")
        s_v = sem("v_ready")
        s_block = sem("blocks_turned")
        s_turn = sem("unit_turned")
        s_hi = sem("unit_hi_ready")
        s_lo = sem("unit_lo_ready")
        s_used = sem("unit_used")
        s_part = sem("partial_kept")
        s_agg = sem("agg_ready")
        s_proj = sem("projected")
        s_neg = sem("neg_part_ready")
        s_elu = sem("elu_parts_ready")
        s_res = sem("residual_steps")
        s_stats = sem("stats_ready")
        s_mv = sem("mean_var_ready")
        s_rstd = sem("rstd_steps")
        s_norm = sem("normed_ready")
        s_out = sem("out_stored")

        def adj_part(row, panel, q):
            rows = adj[PANEL * (row // 2):PANEL * (row // 2 + 1), PANEL * panel + STRIPE * q:PANEL * panel + STRIPE * (q + 1)]
            return rows.rearrange("(b h r) m -> h r b m", h=2, r=B32)[row % 2]

        def nodes_part(t, group, q):
            first = PANEL * (group // 2) + STRIPE * q
            return t[first:first + STRIPE, :].rearrange("(t h c) n -> h c t n", h=2, c=B32)[group % 2]

        def load_chunk(eng, n, qs):
            _, row, panel, _ = chunks[n]
            for q in qs:
                eng.dma_start(raw[n % 2][B32 * q:B32 * (q + 1), :, :], adj_part(row, panel, q)).then_inc(s_raw[n % 2], 16)

        def raw_free(eng, n):
            if units_through[n]:
                eng.wait_ge(s_turn, units_through[n])
            if chunks[n][0] == "A":
                if chunks[n][1] < DEG_ON_DVE:
                    eng.wait_ge(s_degd, n + 1)
                else:
                    eng.wait_ge(s_dega, RB * (n + 1 - PANELS * DEG_ON_DVE))

        def raw_loaded(eng, n):
            eng.wait_ge(s_raw[n % 2], 64 * (n // 2 + 1))

        block = ctx.enter_context(nc.Block())

        @block.sync
        def _(sp):
            def load_x(m):
                if m >= 1 and m <= GROUPS:
                    sp.wait_ge(s_yf, m)
                elif m > GROUPS:
                    sp.wait_ge(s_res, 2 * (m - GROUPS) - 1)
                for q in range(STRIPES):
                    sp.dma_start(x_row[B32 * q:B32 * (q + 1), :, :], nodes_part(x, m % GROUPS, q)).then_inc(s_x, 16)

            for n in range(len(chunks)):
                if n >= 2:
                    raw_free(sp, n - 2)
                load_chunk(sp, n, (0, 1) if n >= 2 else (0, 1, 2, 3))
                if n == 1:
                    sp.dma_start(w_sb[:], w.rearrange("(h c) n -> c h n", h=CH)).then_inc(s_w, 16)
                    sp.dma_start(normed[:, 0:CH, :], W.rearrange("(h c) n -> c h n", h=CH)).then_inc(s_w, 16)
                    sp.dma_start(b_sb[:], b.rearrange("(a n) -> a n", a=1).to_broadcast([P, C])).then_inc(s_w, 16)
                if n % PANELS == 2 and n // PANELS < 2 * GROUPS:
                    load_x(n // PANELS)

        @block.gpsimd
        def _(pool):
            nc.gpsimd.memset(ident[:], 0.0).then_inc(s_zero, 1)
            nc.gpsimd.memset(fold[:], 0.0).then_inc(s_zero, 1)
            nc.gpsimd.memset(minus_half[:], -0.5).then_inc(s_zero, 1)
            pool.wait_ge(s_zero, 3)
            nc.gpsimd.affine_select(out=ident[:], in_=ident[:], compare_op=ALU.not_equal, fill=1.0, base=0,
                                    pattern=[[-1, P]], channel_multiplier=1).then_inc(s_const, 1)
            for q in range(STRIPES):
                if q:
                    pool.wait_ge(s_const, 1 + q)
                nc.gpsimd.affine_select(out=fold[:], in_=fold[:], compare_op=ALU.not_equal, fill=1.0, base=-B32 * q,
                                        pattern=[[-1, B32]], channel_multiplier=1).then_inc(s_const, 1)
            for row in range(GROUPS):
                own = slice(GT * row, GT * (row + 1))
                pool.wait_ge(s_deg, row + 1)
                nc.gpsimd.tensor_tensor(dinv[:, own], deg[:], minus_half[:], ALU.pow).then_inc(s_pow, 1)
                pool.wait_ge(s_pow, row + 1)
                nc.gpsimd.tensor_scalar(ndinv[:, own], dinv[:, own], -1.0, None, ALU.mult).then_inc(s_dinv, 1)
            for i, a in enumerate(rows_done):
                pool.wait_ge(s_mv, GT * (i + 1))
                if i:
                    pool.wait_ge(s_norm, GT * i)
                nc.gpsimd.tensor_scalar(var_eps[:], mean_var[:, :, 1], EPS, None, ALU.add).then_inc(s_rstd, 1)
                nc.gpsimd.tensor_scalar(minus_mean[:], mean_var[:, :, 0], -1.0, None, ALU.mult).then_inc(s_rstd, 1)
                pool.wait_ge(s_rstd, 4 * i + 2)
                nc.gpsimd.tensor_tensor(rstd[:], var_eps[:], minus_half[:], ALU.pow).then_inc(s_rstd, 1)
                pool.wait_ge(s_rstd, 4 * i + 3)
                nc.gpsimd.tensor_tensor(shift[:], minus_mean[:], rstd[:], ALU.mult).then_inc(s_rstd, 1)
                if i >= GROUPS:
                    pool.wait_ge(s_norm, GT * (i + 1))
                    for q in range(STRIPES):
                        pool.dma_start(nodes_part(out, accs[a][1], q), normed[B32 * q:B32 * (q + 1), :, :]).then_inc(s_out, 16)
            pool.wait_ge(s_out, 16 * STRIPES * GROUPS)

        @block.scalar
        def _(act):
            def hi(u):
                act.wait_ge(s_turn, u + 1)
                if u >= 2:
                    act.wait_ge(s_used, u - 1)
                    act.wait_ge(s_lo, u - 1)
                nc.scalar.activation(a_hi[u % 2][:], turned[u % 2][:], ACT.Copy).then_inc(s_hi, 1)

            def deg_part(n):
                _, row, panel, _ = chunks[n]
                for k in range(RB):
                    i = RB * (n - PANELS * DEG_ON_DVE) + k
                    if i >= JUNK:
                        act.wait_ge(s_dega, i - JUNK + 1)
                    nc.scalar.activation(neg[:, i % JUNK, :], raw[n % 2][:, k, :], ACT.Copy,
                                         accum_out=deg_parts[:, row % 2, panel, k:k + 1]).then_inc(s_dega, 1)

            def make_y(row):
                act.wait_ge(s_dinv, row + 1)
                act.wait_ge(s_x, 64 * (row + 1))
                if row:
                    act.wait_ge(s_v, row)
                else:
                    act.wait_ge(s_wt_mm, 1)
                for t in range(GT):
                    ins = nc.scalar.activation(normed[:, t, :], x_row[:, t, :], ACT.Copy,
                                               scale=dinv[:, GT * row + t:GT * row + t + 1])
                ins.then_inc(s_yf, 1)
                act.wait_ge(s_yf, row + 1)
                nc.scalar.activation(v_hi[:, tiles(row), :], normed[:], ACT.Copy).then_inc(s_vhi, 1)

            def keep_partial(a):
                row = accs[a][1]
                act.wait_ge(s_used, accs[a][4] + 1)
                if accs[a][0] == "B":
                    act.wait_ge(s_agg, row + 1)
                nc.scalar.activation(partial[:, row - 1, :, :], acc[a % 3][:], ACT.Copy).then_inc(s_part, 1)

            def elu_parts(a):
                i, row = order_of[a], accs[a][1]
                act.wait_ge(s_proj, i + 1)
                if i:
                    act.wait_ge(s_res, 2 * i)
                    act.wait_ge(s_norm, GT * i)
                for t in range(GT):
                    col = GT * row + t
                    ins = nc.scalar.activation(neg[:, t, :], proj[:, t, :], ACT.Relu, scale=ndinv[:, col:col + 1])
                ins.then_inc(s_neg, 1)
                for t in range(GT):
                    col = GT * row + t
                    nc.scalar.activation(res[:, t, :], proj[:, t, :], ACT.Relu, scale=dinv[:, col:col + 1]).then_inc(s_elu, 1)
                act.wait_ge(s_neg, i + 1)
                nc.scalar.activation(neg[:], neg[:], ACT.Exp, scale=-1.0).then_inc(s_elu, 1)

            def normalise(a):
                i, row = order_of[a], accs[a][1]
                act.wait_ge(s_rstd, 4 * (i + 1))
                if i > GROUPS:
                    act.wait_ge(s_out, 64 * (i - GROUPS))
                else:
                    act.wait_ge(s_v, GROUPS + i)
                for t in range(GT):
                    nc.scalar.activation(normed[:, t, :], res[:, t, :], ACT.Identity, scale=rstd[:, t:t + 1],
                                         bias=shift[:, t:t + 1]).then_inc(s_norm, 1)
                if i < GROUPS:
                    act.wait_ge(s_norm, GT * (i + 1))
                    nc.scalar.activation(v_hi[:, tiles(row), :], normed[:], ACT.Copy).then_inc(s_vhi, 1)

            for n, (name, row, panel, mine) in enumerate(chunks):
                if name == "A" and row >= DEG_ON_DVE:
                    raw_loaded(act, n)
                    deg_part(n)
                for u in mine:
                    hi(u)
                    for a in ended(u, AGG_AT, partials):
                        keep_partial(a)
                    for a in ended(u, ELU_AT, rows_done):
                        if accs[a][2] == 0:
                            elu_parts(a)
                    for a in ended(u, NORM_AT, rows_done):
                        normalise(a)
                if n + 2 < len(chunks):
                    raw_free(act, n)
                    load_chunk(act, n + 2, (2, 3))
                if n % PANELS == 0 and 1 <= n // PANELS <= GROUPS:
                    make_y(n // PANELS - 1)
            for u in range(U, U + NORM_AT + 1):
                for a in ended(u, NORM_AT, rows_done):
                    normalise(a)

        @block.vector
        def _(dve):
            def turn(u):
                name, row, col, n, _ = units[u]
                if u >= 2:
                    dve.wait_ge(s_hi, u - 1)
                    dve.wait_ge(s_lo, u - 1)
                own = name == "B" and row == col
                src = raw[n % 2][:].rearrange("p b (t h c) -> p h t b c", h=2, c=B32)[:, col % 2]
                dst = turned[u % 2][:].rearrange("p t (b r) -> p t b r", r=B32)
                ins = nc.vector.transpose(dst, src)
                ins.then_inc(s_block if own else s_turn, 1)
                if own:
                    dve.wait_ge(s_block, row + 1)
                    for t in range(GT):
                        diag = turned[u % 2][:, t, :].rearrange("p (q t r) -> p t q r", q=STRIPES, r=B32)[:, t]
                        ins = nc.vector.tensor_tensor(diag, diag, ident[:].rearrange("p (q r) -> p q r", r=B32), ALU.add)
                    ins.then_inc(s_turn, 1)

            def lo(u):
                dve.wait_ge(s_hi, u + 1)
                dve.wait_ge(s_turn, u + 1)
                if u >= 2:
                    dve.wait_ge(s_used, u - 1)
                nc.vector.tensor_tensor(a_lo[u % 2][:], turned[u % 2][:], a_hi[u % 2][:].bitcast(F32),
                                        ALU.subtract).then_inc(s_lo, 1)

            def deg_part(n):
                _, row, panel, _ = chunks[n]
                nc.vector.tensor_reduce(deg_parts[:, row % 2, panel, :], raw[n % 2][:], AX_X, ALU.add).then_inc(s_degd, 1)

            def deg_sum(row):
                if row < DEG_ON_DVE:
                    dve.wait_ge(s_degd, PANELS * (row + 1))
                else:
                    dve.wait_ge(s_dega, RB * PANELS * (row + 1 - DEG_ON_DVE))
                if row:
                    dve.wait_ge(s_dmm, row)
                nc.vector.tensor_reduce(deg_sums[:], deg_parts[:, row % 2, :, :].rearrange("p g b -> p b g"),
                                        AX_X, ALU.add).then_inc(s_dsum, 1)

            def deg_row(row):
                dve.wait_ge(s_dmm, row + 1)
                if row:
                    dve.wait_ge(s_pow, row)
                nc.vector.tensor_scalar(deg[:], proj[:, 0, 0:GT], 1.0, None, ALU.add).then_inc(s_deg, 1)

            def v_low(i, row):
                dve.wait_ge(s_vhi, i + 1)
                nc.vector.tensor_tensor(v_lo[:, tiles(row), :], normed[:], v_hi[:, tiles(row), :].bitcast(F32),
                                        ALU.subtract).then_inc(s_v, 1)

            def aggregate(a):
                i, row = order_of[a], accs[a][1]
                dve.wait_ge(s_used, accs[a][4] + 1)
                if i:
                    dve.wait_ge(s_proj, i)
                if row:
                    kept = partial_of[next(k for k in partials if accs[k][1:3] == (row, accs[a][2]))]
                    dve.wait_ge(s_part, kept + 1)
                for h in range(CH):
                    dst = agg[:, h, :].rearrange("p (t q r) -> p q t r", t=GT, q=STRIPES)
                    src = acc[a % 3][:, h, :].rearrange("p (q t r) -> p q t r", t=GT, q=STRIPES)
                    if row:
                        ins = nc.vector.tensor_tensor(dst, src, partial[:, row - 1, h, :].rearrange("p (q t r) -> p q t r", t=GT, q=STRIPES), ALU.add)
                    else:
                        ins = nc.vector.tensor_copy(dst, src)
                ins.then_inc(s_agg, 1)

            def residual(a):
                i, (_, row, layer, _, _) = order_of[a], accs[a]
                if layer == 0:
                    dve.wait_ge(s_elu, (GT + 1) * (i + 1))
                    dve.wait_ge(s_x, 64 * (GROUPS + row + 1))
                    nc.vector.tensor_tensor(res[:], res[:], x_row[:], ALU.add).then_inc(s_res, 1)
                    dve.wait_ge(s_res, 2 * i + 1)
                    nc.vector.scalar_tensor_tensor(out=res[:], in0=neg[:], scalar=-1.0, in1=res[:],
                                                   op0=ALU.add, op1=ALU.add).then_inc(s_res, 1)
                    dve.wait_ge(s_res, 2 * i + 2)
                else:
                    before = 2 * GROUPS + 3 * (i - GROUPS)
                    dve.wait_ge(s_proj, i + 1)
                    dve.wait_ge(s_norm, GT * i)
                    nc.vector.tensor_tensor(res[:], proj[:], b_sb[:].rearrange("p (a n) -> p a n", a=1).to_broadcast([P, GT, C]),
                                            ALU.add).then_inc(s_res, 1)
                    dve.wait_ge(s_res, before + 1)
                    nc.vector.scalar_tensor_tensor(out=res[:], in0=res[:], scalar=0.0, in1=v_hi[:, tiles(row), :].bitcast(F32),
                                                   op0=ALU.max, op1=ALU.add).then_inc(s_res, 1)
                    dve.wait_ge(s_res, before + 2)
                    nc.vector.tensor_tensor(res[:], res[:], v_lo[:, tiles(row), :].bitcast(F32), ALU.add).then_inc(s_res, 1)
                    dve.wait_ge(s_res, before + 3)
                for t in range(GT):
                    nc.vector.bn_stats(stats[:, t, :], res[:, t, :]).then_inc(s_stats, 1)
                if i:
                    dve.wait_ge(s_rstd, 4 * i)
                for t in range(GT):
                    dve.wait_ge(s_stats, GT * i + t + 1)
                    nc.vector.bn_aggr(mean_var[:, t, :], stats[:, t, :]).then_inc(s_mv, 1)

            dve.wait_ge(s_wt_mm, 1)
            nc.vector.tensor_copy(wt_sb[:].rearrange("p h n -> p (h n)"),
                                  proj[:, 0:CH, :].rearrange("p h n -> p (h n)")).then_inc(s_wt, 1)
            dve.wait_ge(s_const, 1)

            for n, (name, row, panel, mine) in enumerate(chunks):
                raw_loaded(dve, n)
                if name == "A" and row < DEG_ON_DVE:
                    deg_part(n)
                for u in mine:
                    turn(u)
                    if u >= 1:
                        lo(u - 1)
                        for a in ended(u - 1, AGG_AT, rows_done):
                            aggregate(a)
                        for a in ended(u - 1, RESIDUAL_AT, rows_done):
                            residual(a)
                        for a in ended(u - 1, NORM_AT, rows_done):
                            if accs[a][2] == 0:
                                v_low(GROUPS + order_of[a], accs[a][1])
                done, at = divmod(n, PANELS)
                if at == PANELS - 1 and done < GROUPS:
                    deg_sum(done)
                if at == 0 and 1 <= done <= GROUPS:
                    deg_row(done - 1)
                if at == 1 and 1 <= done <= GROUPS:
                    v_low(done - 1, done - 1)
            lo(U - 1)
            for u in range(U - 1, U + NORM_AT + 1):
                for a in ended(u, AGG_AT, rows_done):
                    aggregate(a)
                for a in ended(u, RESIDUAL_AT, rows_done):
                    residual(a)

        @block.tensor
        def _(pe):
            pe.wait_ge(s_const, 1)
            pe.wait_ge(s_w, 48)
            for h in range(CH):
                for g in range(CH):
                    ins = pe.transpose(proj[:, h, P * g:P * (g + 1)], normed[:, g, P * h:P * (h + 1)], ident[:])
            ins.then_inc(s_wt_mm, 1)
            pe.wait_ge(s_const, 1 + STRIPES)
            pe.wait_ge(s_wt, 1)

            def fold_degrees(row):
                pe.wait_ge(s_dsum, row + 1)
                if row:
                    pe.wait_ge(s_deg, row)
                for q in range(STRIPES):
                    ins = pe.matmul(proj[B32 * q:B32 * (q + 1), 0, 0:GT], fold[:], deg_sums[:, GT * q:GT * (q + 1)],
                                    start=True, stop=True)
                ins.then_inc(s_dmm, 1)

            def project(a):
                i, layer = order_of[a], accs[a][2]
                pe.wait_ge(s_agg, i + 1)
                if i == 0:
                    pe.wait_ge(s_deg, GROUPS)
                elif i <= GROUPS:
                    pe.wait_ge(s_elu, (GT + 1) * i)
                else:
                    pe.wait_ge(s_res, 2 * GROUPS + 3 * (i - 1 - GROUPS) + 1)
                weights = wt_sb if layer else w_sb
                for t in range(GT):
                    for h in range(CH):
                        ins = pe.matmul(proj[:, t, :], agg[:, h, P * t:P * (t + 1)], weights[:, h, :], start=(h == 0), stop=(h == CH - 1))
                ins.then_inc(s_proj, 1)

            def acc_free(a):
                old = a - 3
                if old < 0:
                    return
                if old in order_of:
                    pe.wait_ge(s_agg, order_of[old] + 1)
                else:
                    pe.wait_ge(s_part, partial_of[old] + 1)

            def product(u):
                name, row, col, n, a = units[u]
                _, _, layer, first, last = accs[a]
                if u == first:
                    acc_free(a)
                pe.wait_ge(s_v, col + 1 if layer == 0 else GROUPS + col + 1)
                pe.wait_ge(s_hi, u + 1)
                pe.wait_ge(s_lo, u + 1)
                tile0 = tiles(col).start
                for t in range(GT):
                    k = tile0 + 2 * t
                    for h in range(CH):
                        ch = slice(P * h, P * (h + 1))
                        dst = acc[a % 3][:, h, :]
                        begin = u == first and t == 0
                        end = u == last and t == GT - 1
                        pe.matmul(dst, v_hi[:, k, ch], a_hi[u % 2][:, t, :], start=begin, stop=False)
                        pe.matmul(dst, v_hi[:, k, ch], a_lo[u % 2][:, t, :], start=False, stop=False)
                        ins = pe.matmul(dst, v_lo[:, k, ch], a_hi[u % 2][:, t, :], start=False, stop=end)
                ins.then_inc(s_used, 1)

            for n, (name, row, panel, mine) in enumerate(chunks):
                for u in mine:
                    product(u)
                    for a in ended(u, PROJECT_AT, rows_done):
                        project(a)
                if name == "A" and panel == PANELS - 1:
                    fold_degrees(row)
            for u in range(U, U + PROJECT_AT + 1):
                for a in ended(u, PROJECT_AT, rows_done):
                    project(a)


_INS = ["x", "adj", "L0_gnn_w", "L1_gnn_W", "L1_gnn_b"]


def kernel(**inputs):
    import numpy as _np
    import concourse.bacc as _bacc
    from concourse import mybir as _mybir
    from concourse.bass_utils import run_bass_kernel_spmd as _run

    nc = _bacc.Bacc("TRN2", target_bir_lowering=False, num_devices=1)
    arrays, args = {}, []
    for name in _INS:
        a = _np.ascontiguousarray(inputs[name])
        arrays[f"in_{name}_dram"] = a
        args.append(nc.dram_tensor(f"in_{name}_dram", a.shape, _mybir.dt.from_np(a.dtype), kind="ExternalInput").ap())
    shape = tuple(inputs["x"].shape)
    args.append(nc.dram_tensor("out_0_dram", shape, _mybir.dt.float32, kind="ExternalOutput").ap())
    gnn_two_layers(nc, *args)
    r = _run(nc, [arrays], core_ids=[0])
    return r.results[0]["out_0_dram"]
```

```python
from contextlib import ExitStack

import concourse.bass as bass
from concourse import mybir

P = 128
B32 = 32
F32 = mybir.dt.float32
F32R = mybir.dt.float32r
ALU = mybir.AluOpType
ACT = mybir.ActivationFunctionType
AX_X = mybir.AxisListType.X


def gnn_two_layers(nc: bass.Bass, x: bass.AP, adj: bass.AP, w: bass.AP, W: bass.AP, b: bass.AP, out: bass.AP):
    N, C = x.shape
    CH = C // P
    STRIPES = P // B32
    STRIPE = 256
    PANEL = STRIPES * STRIPE
    PANELS = N // PANEL
    TPP = STRIPE // B32
    GT = TPP // 2
    GN = GT * P
    GROUPS = 2 * PANELS
    RB = GN // B32
    EPS = 1e-5
    JUNK = 4
    assert (CH, C) == (2, 256) and N == PANELS * PANEL

    def tiles(group):
        first = TPP * (group // 2) + group % 2
        return slice(first, first + 2 * GT - 1, 2)

    chunks = []
    units = []
    accs = []

    def add_chunk(name, row, panel, columns):
        chunks.append((name, row, panel, []))
        for col in columns:
            layer = 0 if name == "A" or (name == "B" and col >= row) else 1
            if not accs or accs[-1][:3] != (name, row, layer):
                accs.append((name, row, layer, len(units), None))
            accs[-1] = accs[-1][:4] + (len(units),)
            chunks[-1][3].append(len(units))
            units.append((name, row, col, len(chunks) - 1, len(accs) - 1))

    ORDER_A = [[1, 2, 3, 0], [1, 2, 3, 0], [1, 2, 3, 0], [2, 0, 3, 1], [2, 0, 3, 1], [3, 0, 1, 2], [0, 3, 1, 2],
               [0, 1, 2, 3]]
    for row in range(GROUPS):
        for panel in ORDER_A[row]:
            add_chunk("A", row, panel, [col for col in (2 * panel, 2 * panel + 1) if col < row])
    for row in range(GROUPS):
        own = row // 2
        for panel in ([*range(own + 1, PANELS), own, *range(own)] if row else range(PANELS)):
            both = (2 * panel, 2 * panel + 1)
            add_chunk("B", row, panel, both[::-1] if panel == own and row % 2 else both)
    for row in reversed(range(GROUPS)):
        for panel in range(row // 2, PANELS):
            add_chunk("C", row, panel, [col for col in (2 * panel, 2 * panel + 1) if col >= row])
    U = len(units)
    FIRST_B = next(n for n, c in enumerate(chunks) if c[0] == "B")
    rows_done = [a for a, s in enumerate(accs) if (s[0], s[2]) in (("B", 0), ("C", 1))]
    partials = [a for a in range(len(accs)) if a not in rows_done]
    order_of = {a: i for i, a in enumerate(rows_done)}
    partial_of = {a: i for i, a in enumerate(partials)}
    buffer_of, before, filled = [], [], []
    for n, c in enumerate(chunks):
        buffer_of.append(n % 3 if c[0] == "A" else n % 2)
        held = [k for k in range(n) if buffer_of[k] == buffer_of[n]]
        before.append(held[-1] if held else None)
        filled.append(len(held) + 1)
    after = {before[n]: n for n in range(len(chunks)) if before[n] is not None}
    units_through = []
    for c in chunks:
        units_through.append((units_through[-1] if units_through else 0) + len(c[3]))

    DVE_BLOCKS = [10, 10, 10, 9, 8, 7, 5, 4]
    act_degs = [PANELS * sum(RB - k for k in DVE_BLOCKS[:row]) for row in range(GROUPS + 1)]

    AGG_AT, PROJECT_AT, ELU_AT, RESIDUAL_AT, MOMENTS_AT, NORM_AT = 2, 1, 3, 4, 5, 6

    def ended(u, lag, which):
        return [a for a in which if accs[a][4] == u - lag]

    with ExitStack() as ctx:
        def sb(name, shape, dt=F32):
            return ctx.enter_context(nc.sbuf_tensor(name, shape, dt))

        def sem(name):
            return ctx.enter_context(nc.semaphore(name))

        v_hi = sb("v_hi", [P, N // P, C], F32R)
        v_lo = sb("v_lo", [P, N // P, C], F32R)
        partial = sb("partial", [P, GROUPS - 1, CH, GN])
        raw = [sb(f"raw{i}", [P, RB, STRIPE]) for i in range(3)]
        turned = [sb(f"turned{i}", [P, GT, GN]) for i in range(2)]
        a_hi = [sb(f"a_hi{i}", [P, GT, GN], F32R) for i in range(2)]
        a_lo = [sb(f"a_lo{i}", [P, GT, GN], F32R) for i in range(2)]
        x_row = sb("x_row", [P, GT, C])
        agg = raw[2][:, 0:4, :].rearrange("p a n -> p (a n)").rearrange("p (h n) -> p h n", h=CH)
        neg, res = raw[2][:, 4:8, :], raw[2][:, 8:12, :]
        junk = sb("junk", [P, JUNK, STRIPE], mybir.dt.bfloat16)
        normed = sb("normed", [P, GT, C])
        w_sb = sb("w_sb", [P, CH, C])
        wt_sb = sb("wt_sb", [P, CH, C])
        b_sb = sb("b_sb", [P, C])
        ident = sb("ident", [P, P])
        fold = sb("fold", [P, B32])
        deg_parts = sb("deg_parts", [P, 2, PANELS, RB])
        deg_sums = sb("deg_sums", [P, RB])
        deg = sb("deg", [P, GT])
        dinv = sb("dinv", [P, N // P])
        ndinv = sb("ndinv", [P, N // P])
        sums = sb("sums", [P, GT])
        squares = sb("squares", [P, GT])
        rstd = sb("rstd", [P, GT])
        var_eps = sb("var_eps", [P, GT])
        minus_mean = sb("minus_mean", [P, GT])
        minus_half = sb("minus_half", [P, GT])
        shift = sb("shift", [P, GT])

        acc = [ctx.enter_context(nc.psum_tensor(f"acc{i}", [P, CH, GN], F32)) for i in range(3)]
        proj = ctx.enter_context(nc.psum_tensor("proj", [P, GT, C], F32))

        s_w = sem("weights_loaded")
        s_x = sem("x_loaded")
        s_raw = [sem(f"raw_loaded{i}") for i in range(3)]
        s_zero = sem("constants_zeroed")
        s_const = sem("constants_made")
        s_wt_mm = sem("wt_turned")
        s_wt = sem("wt_ready")
        s_degd = sem("deg_parts_dve")
        s_dega = sem("deg_parts_act")
        s_dsum = sem("deg_sums_ready")
        s_dmm = sem("deg_folded")
        s_deg = sem("deg_ready")
        s_pow = sem("dinv_made")
        s_dinv = sem("dinv_ready")
        s_yf = sem("y_scaled")
        s_vhi = sem("v_hi_ready")
        s_v = sem("v_ready")
        s_block = sem("blocks_turned")
        s_turn = sem("unit_turned")
        s_hi = sem("unit_hi_ready")
        s_lo = sem("unit_lo_ready")
        s_used = sem("unit_used")
        s_part = sem("partial_kept")
        s_agg = sem("agg_ready")
        s_proj = sem("projected")
        s_neg = sem("neg_part_ready")
        s_elu = sem("elu_parts_ready")
        s_res = sem("residual_steps")
        s_resx = sem("x_added")
        s_sums = sem("sums_ready")
        s_mean = sem("mean_ready")
        s_sq = sem("squares_ready")
        s_rstd = sem("rstd_steps")
        s_norm = sem("normed_ready")
        s_out = sem("out_stored")

        def adj_part(row, panel, q):
            rows = adj[PANEL * (row // 2):PANEL * (row // 2 + 1), PANEL * panel + STRIPE * q:PANEL * panel + STRIPE * (q + 1)]
            return rows.rearrange("(b h r) m -> h r b m", h=2, r=B32)[row % 2]

        def nodes_part(t, group, q):
            first = PANEL * (group // 2) + STRIPE * q
            return t[first:first + STRIPE, :].rearrange("(t h c) n -> h c t n", h=2, c=B32)[group % 2]

        def load_chunk(eng, n, qs):
            _, row, panel, _ = chunks[n]
            for q in qs:
                eng.dma_start(raw[buffer_of[n]][B32 * q:B32 * (q + 1), :, :], adj_part(row, panel, q)).then_inc(s_raw[buffer_of[n]], 16)

        def raw_free(eng, n):
            if units_through[n]:
                eng.wait_ge(s_turn, units_through[n])
            if chunks[n][0] == "A":
                row, place = chunks[n][1], n % PANELS
                eng.wait_ge(s_degd, n + 1)
                eng.wait_ge(s_dega, act_degs[row] + (RB - DVE_BLOCKS[row]) * (place + 1))

        def raw_loaded(eng, n):
            eng.wait_ge(s_raw[buffer_of[n]], 64 * filled[n])

        block = ctx.enter_context(nc.Block())

        @block.sync
        def _(sp):
            def load_x(m):
                if m >= 1 and m <= GROUPS:
                    sp.wait_ge(s_yf, m)
                elif m > GROUPS:
                    sp.wait_ge(s_resx, m - GROUPS)
                for q in range(STRIPES):
                    sp.dma_start(x_row[B32 * q:B32 * (q + 1), :, :], nodes_part(x, m % GROUPS, q)).then_inc(s_x, 16)

            for n in range(len(chunks)):
                if before[n] is not None:
                    raw_free(sp, before[n])
                load_chunk(sp, n, (0, 1) if before[n] is not None else (0, 1, 2, 3))
                if n == 1:
                    sp.dma_start(w_sb[:], w.rearrange("(h c) n -> c h n", h=CH)).then_inc(s_w, 16)
                    sp.dma_start(normed[:, 0:CH, :], W.rearrange("(h c) n -> c h n", h=CH)).then_inc(s_w, 16)
                    sp.dma_start(b_sb[:], b.rearrange("(a n) -> a n", a=1).to_broadcast([P, C])).then_inc(s_w, 16)
                if n % PANELS == 2 and n // PANELS < 2 * GROUPS:
                    load_x(n // PANELS)

        @block.gpsimd
        def _(pool):
            nc.gpsimd.memset(ident[:], 0.0).then_inc(s_zero, 1)
            nc.gpsimd.memset(fold[:], 0.0).then_inc(s_zero, 1)
            nc.gpsimd.memset(minus_half[:], -0.5).then_inc(s_zero, 1)
            pool.wait_ge(s_zero, 3)
            nc.gpsimd.affine_select(out=ident[:], in_=ident[:], compare_op=ALU.not_equal, fill=1.0, base=0,
                                    pattern=[[-1, P]], channel_multiplier=1).then_inc(s_const, 1)
            for q in range(STRIPES):
                if q:
                    pool.wait_ge(s_const, 1 + q)
                nc.gpsimd.affine_select(out=fold[:], in_=fold[:], compare_op=ALU.not_equal, fill=1.0, base=-B32 * q,
                                        pattern=[[-1, B32]], channel_multiplier=1).then_inc(s_const, 1)
            for row in range(GROUPS):
                own = slice(GT * row, GT * (row + 1))
                pool.wait_ge(s_deg, row + 1)
                nc.gpsimd.tensor_tensor(dinv[:, own], deg[:], minus_half[:], ALU.pow).then_inc(s_pow, 1)
                pool.wait_ge(s_pow, row + 1)
                nc.gpsimd.tensor_scalar(ndinv[:, own], dinv[:, own], -1.0, None, ALU.mult).then_inc(s_dinv, 1)
            for i, a in enumerate(rows_done):
                row = accs[a][1]
                if i < GROUPS:
                    pool.wait_ge(s_elu, (GT + 1) * i + GT)
                    pool.wait_ge(s_x, 64 * (GROUPS + row + 1))
                    nc.gpsimd.tensor_tensor(res, res, x_row[:], ALU.add).then_inc(s_resx, 1)
                else:
                    pool.wait_ge(s_v, GROUPS + row + 1)
                    if i > GROUPS:
                        pool.wait_ge(s_res, GROUPS + 2 * (i - GROUPS))
                    nc.gpsimd.tensor_tensor(x_row[:], v_hi[:, tiles(row), :].bitcast(F32), v_lo[:, tiles(row), :].bitcast(F32),
                                            ALU.add).then_inc(s_resx, 1)
                pool.wait_ge(s_sums, GT * (i + 1))
                if i:
                    pool.wait_ge(s_sq, GT * i)
                nc.gpsimd.tensor_scalar(minus_mean[:], sums[:], -1.0 / C, None, ALU.mult).then_inc(s_mean, 1)
                pool.wait_ge(s_sq, GT * (i + 1))
                nc.gpsimd.tensor_scalar(var_eps[:], squares[:], 1.0 / C, EPS, ALU.mult, ALU.add).then_inc(s_rstd, 1)
                pool.wait_ge(s_rstd, 3 * i + 1)
                if i:
                    pool.wait_ge(s_norm, GT * i)
                nc.gpsimd.tensor_tensor(rstd[:], var_eps[:], minus_half[:], ALU.pow).then_inc(s_rstd, 1)
                pool.wait_ge(s_mean, i + 1)
                pool.wait_ge(s_rstd, 3 * i + 2)
                nc.gpsimd.tensor_tensor(shift[:], minus_mean[:], rstd[:], ALU.mult).then_inc(s_rstd, 1)
                if i >= GROUPS:
                    pool.wait_ge(s_norm, GT * (i + 1))
                    for q in range(STRIPES):
                        pool.dma_start(nodes_part(out, accs[a][1], q), normed[B32 * q:B32 * (q + 1), :, :]).then_inc(s_out, 16)
            pool.wait_ge(s_out, 16 * STRIPES * GROUPS)

        @block.scalar
        def _(act):
            def hi(u):
                act.wait_ge(s_turn, u + 1)
                if u >= 2:
                    act.wait_ge(s_used, u - 1)
                    act.wait_ge(s_lo, u - 1)
                nc.scalar.activation(a_hi[u % 2][:], turned[u % 2][:], ACT.Copy).then_inc(s_hi, 1)

            def deg_part(n):
                _, row, panel, _ = chunks[n]
                for k in range(DVE_BLOCKS[row], RB):
                    i = act_degs[row] + (RB - DVE_BLOCKS[row]) * (n % PANELS) + k - DVE_BLOCKS[row]
                    if i >= JUNK:
                        act.wait_ge(s_dega, i - JUNK + 1)
                    nc.scalar.activation(junk[:, i % JUNK, :], raw[buffer_of[n]][:, k, :], ACT.Copy,
                                         accum_out=deg_parts[:, row % 2, panel, k:k + 1]).then_inc(s_dega, 1)

            def make_y(row):
                act.wait_ge(s_dinv, row + 1)
                act.wait_ge(s_x, 64 * (row + 1))
                if row:
                    act.wait_ge(s_v, row)
                else:
                    act.wait_ge(s_wt_mm, 1)
                for t in range(GT):
                    ins = nc.scalar.activation(normed[:, t, :], x_row[:, t, :], ACT.Copy,
                                               scale=dinv[:, GT * row + t:GT * row + t + 1])
                ins.then_inc(s_yf, 1)
                act.wait_ge(s_yf, row + 1)
                nc.scalar.activation(v_hi[:, tiles(row), :], normed[:], ACT.Copy).then_inc(s_vhi, 1)

            def keep_partial(a):
                row = accs[a][1]
                act.wait_ge(s_used, accs[a][4] + 1)
                if accs[a][0] == "B":
                    act.wait_ge(s_agg, row + 1)
                nc.scalar.activation(partial[:, row - 1, :, :], acc[a % 3][:], ACT.Copy).then_inc(s_part, 1)

            def elu_parts(a):
                i, row = order_of[a], accs[a][1]
                act.wait_ge(s_proj, i + 1)
                if i:
                    act.wait_ge(s_res, i)
                    act.wait_ge(s_norm, GT * i)
                else:
                    act.wait_ge(s_turn, units_through[FIRST_B - 1])
                    act.wait_ge(s_degd, FIRST_B)
                for t in range(GT):
                    col = GT * row + t
                    ins = nc.scalar.activation(neg[:, t, :], proj[:, t, :], ACT.Relu, scale=ndinv[:, col:col + 1])
                ins.then_inc(s_neg, 1)
                for t in range(GT):
                    col = GT * row + t
                    nc.scalar.activation(res[:, t, :], proj[:, t, :], ACT.Relu, scale=dinv[:, col:col + 1]).then_inc(s_elu, 1)
                act.wait_ge(s_neg, i + 1)
                nc.scalar.activation(neg, neg, ACT.Exp, scale=-1.0).then_inc(s_elu, 1)

            def moments(a):
                i = order_of[a]
                act.wait_ge(s_res, i + 1 if i < GROUPS else GROUPS + 2 * (i - GROUPS + 1))
                if i:
                    act.wait_ge(s_mean, i)
                for t in range(GT):
                    nc.scalar.activation(neg[:, t, :], res[:, t, :], ACT.Copy, accum_out=sums[:, t:t + 1]).then_inc(s_sums, 1)
                act.wait_ge(s_sums, GT * (i + 1))
                act.wait_ge(s_mean, i + 1)
                if i:
                    act.wait_ge(s_rstd, 3 * i - 2)
                for t in range(GT):
                    nc.scalar.activation(neg[:, t, :], res[:, t, :], ACT.Square, bias=minus_mean[:, t:t + 1],
                                         accum_out=squares[:, t:t + 1]).then_inc(s_sq, 1)

            def normalise(a):
                i, row = order_of[a], accs[a][1]
                act.wait_ge(s_rstd, 3 * (i + 1))
                if i > GROUPS:
                    act.wait_ge(s_out, 64 * (i - GROUPS))
                else:
                    act.wait_ge(s_v, GROUPS + i)
                for t in range(GT):
                    nc.scalar.activation(normed[:, t, :], res[:, t, :], ACT.Identity, scale=rstd[:, t:t + 1],
                                         bias=shift[:, t:t + 1]).then_inc(s_norm, 1)
                if i < GROUPS:
                    act.wait_ge(s_norm, GT * (i + 1))
                    nc.scalar.activation(v_hi[:, tiles(row), :], normed[:], ACT.Copy).then_inc(s_vhi, 1)

            for n, (name, row, panel, mine) in enumerate(chunks):
                for u in mine:
                    hi(u)
                    for a in ended(u, AGG_AT, partials):
                        keep_partial(a)
                    for a in ended(u, ELU_AT, rows_done):
                        if accs[a][2] == 0:
                            elu_parts(a)
                    for a in ended(u, MOMENTS_AT, rows_done):
                        moments(a)
                    for a in ended(u, NORM_AT, rows_done):
                        normalise(a)
                if name == "A":
                    raw_loaded(act, n)
                    deg_part(n)
                if n in after:
                    raw_free(act, n)
                    load_chunk(act, after[n], (2, 3))
                if n % PANELS == 0 and 1 <= n // PANELS <= GROUPS:
                    make_y(n // PANELS - 1)
            for u in range(U, U + NORM_AT + 1):
                for a in ended(u, MOMENTS_AT, rows_done):
                    moments(a)
                for a in ended(u, NORM_AT, rows_done):
                    normalise(a)

        @block.vector
        def _(dve):
            def turn(u):
                name, row, col, n, _ = units[u]
                if u >= 2:
                    dve.wait_ge(s_hi, u - 1)
                    dve.wait_ge(s_lo, u - 1)
                own = name == "B" and row == col
                src = raw[buffer_of[n]][:].rearrange("p b (t h c) -> p h t b c", h=2, c=B32)[:, col % 2]
                dst = turned[u % 2][:].rearrange("p t (b r) -> p t b r", r=B32)
                ins = nc.vector.transpose(dst, src)
                ins.then_inc(s_block if own else s_turn, 1)
                if own:
                    dve.wait_ge(s_block, row + 1)
                    for t in range(GT):
                        diag = turned[u % 2][:, t, :].rearrange("p (q t r) -> p t q r", q=STRIPES, r=B32)[:, t]
                        ins = nc.vector.tensor_tensor(diag, diag, ident[:].rearrange("p (q r) -> p q r", r=B32), ALU.add)
                    ins.then_inc(s_turn, 1)

            def lo(u):
                dve.wait_ge(s_hi, u + 1)
                dve.wait_ge(s_turn, u + 1)
                if u >= 2:
                    dve.wait_ge(s_used, u - 1)
                nc.vector.tensor_tensor(a_lo[u % 2][:], turned[u % 2][:], a_hi[u % 2][:].bitcast(F32),
                                        ALU.subtract).then_inc(s_lo, 1)

            def deg_part(n):
                _, row, panel, _ = chunks[n]
                mine = slice(0, DVE_BLOCKS[row])
                nc.vector.tensor_reduce(deg_parts[:, row % 2, panel, mine], raw[buffer_of[n]][:, mine, :], AX_X,
                                        ALU.add).then_inc(s_degd, 1)

            def deg_sum(row):
                dve.wait_ge(s_degd, PANELS * (row + 1))
                dve.wait_ge(s_dega, act_degs[row + 1])
                if row:
                    dve.wait_ge(s_dmm, row)
                nc.vector.tensor_reduce(deg_sums[:], deg_parts[:, row % 2, :, :].rearrange("p g b -> p b g"),
                                        AX_X, ALU.add).then_inc(s_dsum, 1)

            def deg_row(row):
                dve.wait_ge(s_dmm, row + 1)
                if row:
                    dve.wait_ge(s_pow, row)
                nc.vector.tensor_scalar(deg[:], proj[:, 0, 0:GT], 1.0, None, ALU.add).then_inc(s_deg, 1)

            def v_low(i, row):
                dve.wait_ge(s_vhi, i + 1)
                nc.vector.tensor_tensor(v_lo[:, tiles(row), :], normed[:], v_hi[:, tiles(row), :].bitcast(F32),
                                        ALU.subtract).then_inc(s_v, 1)

            def aggregate(a):
                i, row = order_of[a], accs[a][1]
                dve.wait_ge(s_used, accs[a][4] + 1)
                if i:
                    dve.wait_ge(s_proj, i)
                else:
                    dve.wait_ge(s_dega, act_degs[GROUPS])
                if row:
                    kept = partial_of[next(k for k in partials if accs[k][1:3] == (row, accs[a][2]))]
                    dve.wait_ge(s_part, kept + 1)
                for h in range(CH):
                    dst = agg[:, h, :].rearrange("p (t q r) -> p q t r", t=GT, q=STRIPES)
                    src = acc[a % 3][:, h, :].rearrange("p (q t r) -> p q t r", t=GT, q=STRIPES)
                    if row:
                        ins = nc.vector.tensor_tensor(dst, src, partial[:, row - 1, h, :].rearrange("p (q t r) -> p q t r", t=GT, q=STRIPES), ALU.add)
                    else:
                        ins = nc.vector.tensor_copy(dst, src)
                ins.then_inc(s_agg, 1)

            def residual(a):
                i, (_, row, layer, _, _) = order_of[a], accs[a]
                if layer == 0:
                    dve.wait_ge(s_elu, (GT + 1) * (i + 1))
                    dve.wait_ge(s_resx, i + 1)
                    nc.vector.scalar_tensor_tensor(out=res, in0=neg, scalar=-1.0, in1=res,
                                                   op0=ALU.add, op1=ALU.add).then_inc(s_res, 1)
                else:
                    dve.wait_ge(s_proj, i + 1)
                    dve.wait_ge(s_norm, GT * i)
                    nc.vector.tensor_tensor(res, proj[:], b_sb[:].rearrange("p (a n) -> p a n", a=1).to_broadcast([P, GT, C]),
                                            ALU.add).then_inc(s_res, 1)
                    dve.wait_ge(s_resx, i + 1)
                    dve.wait_ge(s_res, GROUPS + 2 * (i - GROUPS) + 1)
                    nc.vector.scalar_tensor_tensor(out=res, in0=res, scalar=0.0, in1=x_row[:],
                                                   op0=ALU.max, op1=ALU.add).then_inc(s_res, 1)

            def low_and_later(u):
                if lows_done[0] > u:
                    return
                lows_done[0] = u + 1
                lo(u)
                for a in ended(u, AGG_AT, rows_done):
                    aggregate(a)
                for a in ended(u, RESIDUAL_AT, rows_done):
                    residual(a)
                for a in ended(u, NORM_AT, rows_done):
                    if accs[a][2] == 0:
                        v_low(GROUPS + order_of[a], accs[a][1])

            lows_done = [0]

            dve.wait_ge(s_wt_mm, 1)
            nc.vector.tensor_copy(wt_sb[:].rearrange("p h n -> p (h n)"),
                                  proj[:, 0:CH, :].rearrange("p h n -> p (h n)")).then_inc(s_wt, 1)
            dve.wait_ge(s_const, 1)

            for n, (name, row, panel, mine) in enumerate(chunks):
                raw_loaded(dve, n)
                for u in mine:
                    turn(u)
                    if u != mine[0] or name != "A":
                        low_and_later(u - 1)
                if name == "A":
                    deg_part(n)
                    if mine:
                        low_and_later(mine[-1])
                done, at = divmod(n, PANELS)
                if at == PANELS - 1 and done < GROUPS:
                    deg_sum(done)
                if at == 0 and 1 <= done <= GROUPS:
                    deg_row(done - 1)
                if at == 1 and 1 <= done <= GROUPS:
                    v_low(done - 1, done - 1)
            lo(U - 1)
            for u in range(U - 1, U + NORM_AT + 1):
                for a in ended(u, AGG_AT, rows_done):
                    aggregate(a)
                for a in ended(u, RESIDUAL_AT, rows_done):
                    residual(a)

        @block.tensor
        def _(pe):
            pe.wait_ge(s_const, 1)
            pe.wait_ge(s_w, 48)
            for h in range(CH):
                for g in range(CH):
                    ins = pe.transpose(proj[:, h, P * g:P * (g + 1)], normed[:, g, P * h:P * (h + 1)], ident[:])
            ins.then_inc(s_wt_mm, 1)
            pe.wait_ge(s_const, 1 + STRIPES)
            pe.wait_ge(s_wt, 1)

            def fold_degrees(row):
                pe.wait_ge(s_dsum, row + 1)
                if row:
                    pe.wait_ge(s_deg, row)
                for q in range(STRIPES):
                    ins = pe.matmul(proj[B32 * q:B32 * (q + 1), 0, 0:GT], fold[:], deg_sums[:, GT * q:GT * (q + 1)],
                                    start=True, stop=True)
                ins.then_inc(s_dmm, 1)

            def project(a):
                i, layer = order_of[a], accs[a][2]
                pe.wait_ge(s_agg, i + 1)
                if i == 0:
                    pe.wait_ge(s_deg, GROUPS)
                elif i <= GROUPS:
                    pe.wait_ge(s_elu, (GT + 1) * i)
                else:
                    pe.wait_ge(s_res, GROUPS + 2 * (i - 1 - GROUPS) + 1)
                weights = wt_sb if layer else w_sb
                for t in range(GT):
                    for h in range(CH):
                        ins = pe.matmul(proj[:, t, :], agg[:, h, P * t:P * (t + 1)], weights[:, h, :], start=(h == 0), stop=(h == CH - 1))
                ins.then_inc(s_proj, 1)

            def acc_free(a):
                old = a - 3
                if old < 0:
                    return
                if old in order_of:
                    pe.wait_ge(s_agg, order_of[old] + 1)
                else:
                    pe.wait_ge(s_part, partial_of[old] + 1)

            def product(u):
                name, row, col, n, a = units[u]
                _, _, layer, first, last = accs[a]
                if u == first:
                    acc_free(a)
                pe.wait_ge(s_v, col + 1 if layer == 0 else GROUPS + col + 1)
                pe.wait_ge(s_hi, u + 1)
                pe.wait_ge(s_lo, u + 1)
                tile0 = tiles(col).start
                for t in range(GT):
                    k = tile0 + 2 * t
                    for h in range(CH):
                        ch = slice(P * h, P * (h + 1))
                        dst = acc[a % 3][:, h, :]
                        begin = u == first and t == 0
                        end = u == last and t == GT - 1
                        pe.matmul(dst, v_hi[:, k, ch], a_hi[u % 2][:, t, :], start=begin, stop=False)
                        pe.matmul(dst, v_hi[:, k, ch], a_lo[u % 2][:, t, :], start=False, stop=False)
                        ins = pe.matmul(dst, v_lo[:, k, ch], a_hi[u % 2][:, t, :], start=False, stop=end)
                ins.then_inc(s_used, 1)

            for n, (name, row, panel, mine) in enumerate(chunks):
                for u in mine:
                    product(u)
                    for a in ended(u, PROJECT_AT, rows_done):
                        project(a)
                if name == "A" and n % PANELS == PANELS - 1:
                    fold_degrees(row)
            for u in range(U, U + PROJECT_AT + 1):
                for a in ended(u, PROJECT_AT, rows_done):
                    project(a)


_INS = ["x", "adj", "L0_gnn_w", "L1_gnn_W", "L1_gnn_b"]


def kernel(**inputs):
    import numpy as _np
    import concourse.bacc as _bacc
    from concourse import mybir as _mybir
    from concourse.bass_utils import run_bass_kernel_spmd as _run

    nc = _bacc.Bacc("TRN2", target_bir_lowering=False, num_devices=1)
    arrays, args = {}, []
    for name in _INS:
        a = _np.ascontiguousarray(inputs[name])
        arrays[f"in_{name}_dram"] = a
        args.append(nc.dram_tensor(f"in_{name}_dram", a.shape, _mybir.dt.from_np(a.dtype), kind="ExternalInput").ap())
    shape = tuple(inputs["x"].shape)
    args.append(nc.dram_tensor("out_0_dram", shape, _mybir.dt.float32, kind="ExternalOutput").ap())
    gnn_two_layers(nc, *args)
    r = _run(nc, [arrays], core_ids=[0])
    return r.results[0]["out_0_dram"]
```

```python
from contextlib import ExitStack

import concourse.bass as bass
from concourse import mybir

P = 128
B32 = 32
F32 = mybir.dt.float32
F32R = mybir.dt.float32r
ALU = mybir.AluOpType
ACT = mybir.ActivationFunctionType
AX_X = mybir.AxisListType.X


def gnn_two_layers(nc: bass.Bass, x: bass.AP, adj: bass.AP, w: bass.AP, W: bass.AP, b: bass.AP, out: bass.AP):
    N, C = x.shape
    CH = C // P
    STRIPES = P // B32
    STRIPE = 256
    PANEL = STRIPES * STRIPE
    PANELS = N // PANEL
    TPP = STRIPE // B32
    GT = TPP // 2
    GN = GT * P
    GROUPS = 2 * PANELS
    RB = GN // B32
    EPS = 1e-5
    JUNK = 2
    assert (CH, C) == (2, 256) and N == PANELS * PANEL

    def tiles(group):
        first = TPP * (group // 2) + group % 2
        return slice(first, first + 2 * GT - 1, 2)

    chunks = []
    units = []
    accs = []

    def add_chunk(name, row, panel, columns):
        chunks.append((name, row, panel, []))
        for col in columns:
            layer = 0 if name == "A" or (name == "B" and col >= row) else 1
            if not accs or accs[-1][:3] != (name, row, layer):
                accs.append((name, row, layer, len(units), None))
            accs[-1] = accs[-1][:4] + (len(units),)
            chunks[-1][3].append(len(units))
            units.append((name, row, col, len(chunks) - 1, len(accs) - 1))

    DIAGONALS = 1
    ORDER_A = [[1, 2, 3, 0], [1, 2, 3, 0], [2, 0, 3, 1], [2, 0, 3, 1], [2, 0, 3, 1], [0, 3, 1, 2], [0, 3, 1, 2],
               [0, 1, 2, 3]]
    for row in range(GROUPS):
        for panel in ORDER_A[row]:
            add_chunk("A", row, panel, [col for col in (2 * panel, 2 * panel + 1)
                                        if col < row or col == row < DIAGONALS])
    for row in range(GROUPS):
        own = row // 2
        for panel in ([*range(own + 1, PANELS), own, *range(own)] if row else range(PANELS)):
            both = [col for col in (2 * panel, 2 * panel + 1) if not col == row < DIAGONALS]
            add_chunk("B", row, panel, both[::-1] if panel == own and row % 2 else both)
    for row in reversed(range(GROUPS)):
        for panel in range(row // 2, PANELS):
            add_chunk("C", row, panel, [col for col in (2 * panel, 2 * panel + 1) if col >= row])
    U = len(units)
    FIRST_B = next(n for n, c in enumerate(chunks) if c[0] == "B")
    rows_done = [a for a, s in enumerate(accs) if (s[0], s[2]) in (("B", 0), ("C", 1))]
    partials = [a for a in range(len(accs)) if a not in rows_done]
    bank_of = [a % 2 if s[0] == "A" else a % 3 for a, s in enumerate(accs)]
    acc_before = [next((k for k in reversed(range(a)) if bank_of[k] == bank_of[a]), None) for a in range(len(accs))]
    order_of = {a: i for i, a in enumerate(rows_done)}
    partial_of = {a: i for i, a in enumerate(partials)}
    THIRD = next(n for n, c in enumerate(chunks) if c[0] == "B" and n % 3 == 2)
    buffer_of, before, filled = [], [], []
    for n, c in enumerate(chunks):
        buffer_of.append(n % 3 if n <= THIRD + 2 else (n - THIRD - 1) % 2)
        held = [k for k in range(n) if buffer_of[k] == buffer_of[n]]
        before.append(held[-1] if held else None)
        filled.append(len(held) + 1)
    after = {before[n]: n for n in range(len(chunks)) if before[n] is not None}
    units_through = []
    for c in chunks:
        units_through.append((units_through[-1] if units_through else 0) + len(c[3]))

    DVE_BLOCKS = [10, 10, 10, 9, 9, 8, 7, 6]
    last_in_a = [max((u for u in range(U) if units[u][0] == "A" and units[u][1] == row), default=None)
                 for row in range(GROUPS)]
    act_degs = [PANELS * sum(RB - k for k in DVE_BLOCKS[:row]) for row in range(GROUPS + 1)]

    Y_AT = 2
    AGG_AT, PROJECT_AT, ELU_AT, RESIDUAL_AT, MOMENTS_AT, NORM_AT = 2, 2, 4, 5, 6, 7

    def ended(u, lag, which):
        return [a for a in which if accs[a][4] == u - lag]

    def halves_of(u, half):
        return 2 * u + half + 1

    HALVES = [(0, slice(0, GT // 2)), (1, slice(GT // 2, GT))]

    with ExitStack() as ctx:
        def sb(name, shape, dt=F32):
            return ctx.enter_context(nc.sbuf_tensor(name, shape, dt))

        def sem(name):
            return ctx.enter_context(nc.semaphore(name))

        v_hi = sb("v_hi", [P, N // P, C], F32R)
        v_lo = sb("v_lo", [P, N // P, C], F32R)
        partial = sb("partial", [P, GROUPS, CH, GN])
        raw = [sb(f"raw{i}", [P, RB, STRIPE]) for i in range(3)]
        turned = [sb(f"turned{i}", [P, GT, GN]) for i in range(2)]
        a_hi = [sb(f"a_hi{i}", [P, GT, GN], F32R) for i in range(2)]
        a_lo = [sb(f"a_lo{i}", [P, GT, GN], F32R) for i in range(2)]
        x_row = sb("x_row", [P, GT, C])
        agg = raw[2][:, 0:4, :].rearrange("p a n -> p (a n)").rearrange("p (h n) -> p h n", h=CH)
        neg, res = raw[2][:, 4:8, :], raw[2][:, 8:12, :]
        normed = sb("normed", [P, GT, C])
        w_sb = sb("w_sb", [P, CH, C])
        wt_sb = sb("wt_sb", [P, CH, C])
        b_sb = sb("b_sb", [P, C])
        ident = sb("ident", [P, P])
        fold = sb("fold", [P, B32])
        deg_parts = sb("deg_parts", [P, 2, PANELS, RB])
        deg_sums = sb("deg_sums", [P, RB])
        deg = sb("deg", [P, GT])
        dinv = sb("dinv", [P, N // P])
        ndinv = sb("ndinv", [P, N // P])
        sums = sb("sums", [P, GT])
        squares = sb("squares", [P, GT])
        rstd = sb("rstd", [P, GT])
        var_eps = sb("var_eps", [P, GT])
        minus_mean = sb("minus_mean", [P, GT])
        minus_half = sb("minus_half", [P, GT])
        shift = sb("shift", [P, GT])

        acc = [ctx.enter_context(nc.psum_tensor(f"acc{i}", [P, CH, GN], F32)) for i in range(3)]
        junk = acc[2][:, 1, :].rearrange("p (j m) -> p j m", j=JUNK)
        proj = ctx.enter_context(nc.psum_tensor("proj", [P, GT, C], F32))

        s_w = sem("weights_loaded")
        s_x = sem("x_loaded")
        s_raw = [sem(f"raw_loaded{i}") for i in range(3)]
        s_zero = sem("constants_zeroed")
        s_const = sem("constants_made")
        s_wt_mm = sem("wt_turned")
        s_wt = sem("wt_ready")
        s_degd = sem("deg_parts_dve")
        s_dega = sem("deg_parts_act")
        s_dsum = sem("deg_sums_ready")
        s_dmm = sem("deg_folded")
        s_deg = sem("deg_ready")
        s_pow = sem("dinv_made")
        s_dinv = sem("dinv_ready")
        s_xt_mm = sem("x_turned")
        s_xt = sem("xt_ready")
        s_xw = sem("xw_ready")
        s_yf = sem("y_scaled")
        s_vhi = sem("v_hi_ready")
        s_v = sem("v_ready")
        s_block = sem("blocks_turned")
        s_turn = sem("unit_turned")
        s_hi = sem("hi_halves_ready")
        s_lo = sem("lo_halves_ready")
        s_used = sem("halves_used")
        s_part = sem("partial_kept")
        s_agg = sem("agg_ready")
        s_proj = sem("projected")
        s_neg = sem("neg_part_ready")
        s_elu = sem("elu_parts_ready")
        s_res = sem("residual_steps")
        s_resx = sem("x_added")
        s_sums = sem("sums_ready")
        s_mean = sem("mean_ready")
        s_sq = sem("squares_ready")
        s_rstd = sem("rstd_steps")
        s_norm = sem("normed_ready")
        s_out = sem("out_stored")

        def adj_part(row, panel, q):
            rows = adj[PANEL * (row // 2):PANEL * (row // 2 + 1), PANEL * panel + STRIPE * q:PANEL * panel + STRIPE * (q + 1)]
            return rows.rearrange("(b h r) m -> h r b m", h=2, r=B32)[row % 2]

        def nodes_part(t, group, q):
            first = PANEL * (group // 2) + STRIPE * q
            return t[first:first + STRIPE, :].rearrange("(t h c) n -> h c t n", h=2, c=B32)[group % 2]

        def load_chunk(eng, n, qs):
            _, row, panel, _ = chunks[n]
            for q in qs:
                eng.dma_start(raw[buffer_of[n]][B32 * q:B32 * (q + 1), :, :], adj_part(row, panel, q)).then_inc(s_raw[buffer_of[n]], 16)

        def raw_free(eng, n):
            if units_through[n]:
                eng.wait_ge(s_turn, units_through[n])
            if chunks[n][0] == "A":
                row, place = chunks[n][1], n % PANELS
                eng.wait_ge(s_degd, n + 1)
                eng.wait_ge(s_dega, act_degs[row] + (RB - DVE_BLOCKS[row]) * (place + 1))

        def raw_loaded(eng, n):
            eng.wait_ge(s_raw[buffer_of[n]], 64 * filled[n])

        block = ctx.enter_context(nc.Block())

        @block.sync
        def _(sp):
            def load_x(m):
                if m >= 1 and m <= GROUPS:
                    sp.wait_ge(s_xw, m)
                elif m > GROUPS:
                    sp.wait_ge(s_resx, m - GROUPS)
                for q in range(STRIPES):
                    sp.dma_start(x_row[B32 * q:B32 * (q + 1), :, :], nodes_part(x, m % GROUPS, q)).then_inc(s_x, 16)

            x_loads_after = [[] for _ in chunks]
            for m in range(2 * GROUPS):
                if m <= GROUPS:
                    n = PANELS * m + 2
                else:
                    n = units[accs[rows_done[m - GROUPS - 1]][4] + RESIDUAL_AT + 0][3] + 2
                x_loads_after[n].append(m)
            for n in range(len(chunks)):
                if before[n] is not None:
                    raw_free(sp, before[n])
                load_chunk(sp, n, (0, 2, 1, 3))
                if n == 1:
                    sp.dma_start(w_sb[:], w.rearrange("(h c) n -> c h n", h=CH)).then_inc(s_w, 16)
                    sp.dma_start(normed[:, 0:CH, :], W.rearrange("(h c) n -> c h n", h=CH)).then_inc(s_w, 16)
                    sp.dma_start(b_sb[:], b.rearrange("(a n) -> a n", a=1).to_broadcast([P, C])).then_inc(s_w, 16)
                for m in x_loads_after[n]:
                    load_x(m)

        @block.gpsimd
        def _(pool):
            nc.gpsimd.memset(ident[:], 0.0).then_inc(s_zero, 1)
            nc.gpsimd.memset(fold[:], 0.0).then_inc(s_zero, 1)
            nc.gpsimd.memset(minus_half[:], -0.5).then_inc(s_zero, 1)
            pool.wait_ge(s_zero, 3)
            nc.gpsimd.affine_select(out=ident[:], in_=ident[:], compare_op=ALU.not_equal, fill=1.0, base=0,
                                    pattern=[[-1, P]], channel_multiplier=1).then_inc(s_const, 1)
            for q in range(STRIPES):
                if q:
                    pool.wait_ge(s_const, 1 + q)
                nc.gpsimd.affine_select(out=fold[:], in_=fold[:], compare_op=ALU.not_equal, fill=1.0, base=-B32 * q,
                                        pattern=[[-1, B32]], channel_multiplier=1).then_inc(s_const, 1)
            for row in range(GROUPS):
                own = slice(GT * row, GT * (row + 1))
                pool.wait_ge(s_deg, row + 1)
                nc.gpsimd.tensor_tensor(dinv[:, own], deg[:], minus_half[:], ALU.pow).then_inc(s_pow, 1)
                pool.wait_ge(s_pow, row + 1)
                nc.gpsimd.tensor_scalar(ndinv[:, own], dinv[:, own], -1.0, None, ALU.mult).then_inc(s_dinv, 1)
            for i, a in enumerate(rows_done):
                row = accs[a][1]
                if i < GROUPS:
                    pool.wait_ge(s_elu, (GT + 1) * i + GT)
                    pool.wait_ge(s_x, 64 * (GROUPS + row + 1))
                    nc.gpsimd.tensor_tensor(res, res, x_row[:], ALU.add).then_inc(s_resx, 1)
                else:
                    pool.wait_ge(s_v, GROUPS + row + 1)
                    if i > GROUPS:
                        pool.wait_ge(s_res, GROUPS + 2 * (i - GROUPS))
                    nc.gpsimd.tensor_tensor(x_row[:], v_hi[:, tiles(row), :].bitcast(F32), v_lo[:, tiles(row), :].bitcast(F32),
                                            ALU.add).then_inc(s_resx, 1)
                pool.wait_ge(s_sums, GT * (i + 1))
                if i:
                    pool.wait_ge(s_sq, GT * i)
                nc.gpsimd.tensor_scalar(minus_mean[:], sums[:], -1.0 / C, None, ALU.mult).then_inc(s_mean, 1)
                pool.wait_ge(s_sq, GT * (i + 1))
                nc.gpsimd.tensor_scalar(var_eps[:], squares[:], 1.0 / C, EPS, ALU.mult, ALU.add).then_inc(s_rstd, 1)
                pool.wait_ge(s_rstd, 3 * i + 1)
                if i:
                    pool.wait_ge(s_norm, GT * i)
                nc.gpsimd.tensor_tensor(rstd[:], var_eps[:], minus_half[:], ALU.pow).then_inc(s_rstd, 1)
                pool.wait_ge(s_mean, i + 1)
                pool.wait_ge(s_rstd, 3 * i + 2)
                nc.gpsimd.tensor_tensor(shift[:], minus_mean[:], rstd[:], ALU.mult).then_inc(s_rstd, 1)

        @block.scalar
        def _(act):
            def hi(u):
                act.wait_ge(s_turn, u + 1)
                for half, part in HALVES:
                    if u >= 2:
                        act.wait_ge(s_used, halves_of(u - 2, half))
                        act.wait_ge(s_lo, halves_of(u - 2, half))
                    nc.scalar.activation(a_hi[u % 2][:, part, :], turned[u % 2][:, part, :],
                                         ACT.Copy).then_inc(s_hi, 1)

            def deg_part(n):
                _, row, panel, _ = chunks[n]
                for k in range(DVE_BLOCKS[row], RB):
                    i = act_degs[row] + (RB - DVE_BLOCKS[row]) * (n % PANELS) + k - DVE_BLOCKS[row]
                    if i >= JUNK:
                        act.wait_ge(s_dega, i - JUNK + 1)
                    nc.scalar.activation(junk[:, i % JUNK, :], raw[buffer_of[n]][:, k, :], ACT.Copy,
                                         accum_out=deg_parts[:, row % 2, panel, k:k + 1]).then_inc(s_dega, 1)

            def make_y(row):
                act.wait_ge(s_dinv, row + 1)
                act.wait_ge(s_xw, row + 1)
                if row:
                    act.wait_ge(s_v, row)
                for t in range(GT):
                    ins = nc.scalar.activation(normed[:, t, :], proj[:, t, :], ACT.Copy,
                                               scale=dinv[:, GT * row + t:GT * row + t + 1])
                ins.then_inc(s_yf, 1)
                act.wait_ge(s_yf, row + 1)
                nc.scalar.activation(v_hi[:, tiles(row), :], normed[:], ACT.Copy).then_inc(s_vhi, 1)

            def keep_xt(row):
                act.wait_ge(s_xt_mm, row + 1)
                nc.scalar.activation(x_row[:].rearrange("p t n -> p (t n)"), proj[:].rearrange("p t n -> p (t n)"),
                                     ACT.Copy).then_inc(s_xt, 1)

            def keep_partial(a):
                row = accs[a][1]
                act.wait_ge(s_used, halves_of(accs[a][4], 1))
                if accs[a][0] == "B":
                    act.wait_ge(s_agg, row + 1)
                nc.scalar.activation(partial[:, row, :, :], acc[bank_of[a]][:], ACT.Copy).then_inc(s_part, 1)

            def elu_parts(a):
                i, row = order_of[a], accs[a][1]
                act.wait_ge(s_proj, i + 1)
                if i:
                    act.wait_ge(s_res, i)
                    act.wait_ge(s_norm, GT * i)
                else:
                    act.wait_ge(s_turn, units_through[THIRD])
                    act.wait_ge(s_degd, FIRST_B)
                for t in range(GT):
                    col = GT * row + t
                    ins = nc.scalar.activation(neg[:, t, :], proj[:, t, :], ACT.Relu, scale=ndinv[:, col:col + 1])
                ins.then_inc(s_neg, 1)
                for t in range(GT):
                    col = GT * row + t
                    nc.scalar.activation(res[:, t, :], proj[:, t, :], ACT.Relu, scale=dinv[:, col:col + 1]).then_inc(s_elu, 1)
                act.wait_ge(s_neg, i + 1)
                nc.scalar.activation(neg, neg, ACT.Exp, scale=-1.0).then_inc(s_elu, 1)

            def moments(a):
                i = order_of[a]
                act.wait_ge(s_res, i + 1 if i < GROUPS else GROUPS + 2 * (i - GROUPS + 1))
                if i:
                    act.wait_ge(s_mean, i)
                for t in range(GT):
                    nc.scalar.activation(neg[:, t, :], res[:, t, :], ACT.Copy, accum_out=sums[:, t:t + 1]).then_inc(s_sums, 1)
                act.wait_ge(s_sums, GT * (i + 1))
                act.wait_ge(s_mean, i + 1)
                if i:
                    act.wait_ge(s_rstd, 3 * i - 2)
                for t in range(GT):
                    nc.scalar.activation(neg[:, t, :], res[:, t, :], ACT.Square, bias=minus_mean[:, t:t + 1],
                                         accum_out=squares[:, t:t + 1]).then_inc(s_sq, 1)

            def normalise(a):
                i, row = order_of[a], accs[a][1]
                act.wait_ge(s_rstd, 3 * (i + 1))
                if i > GROUPS:
                    act.wait_ge(s_out, 64 * (i - GROUPS))
                else:
                    act.wait_ge(s_v, GROUPS + i)
                for t in range(GT):
                    nc.scalar.activation(normed[:, t, :], res[:, t, :], ACT.Identity, scale=rstd[:, t:t + 1],
                                         bias=shift[:, t:t + 1]).then_inc(s_norm, 1)
                act.wait_ge(s_norm, GT * (i + 1))
                if i < GROUPS:
                    nc.scalar.activation(v_hi[:, tiles(row), :], normed[:], ACT.Copy).then_inc(s_vhi, 1)
                else:
                    for q in range(STRIPES):
                        act.dma_start(nodes_part(out, row, q), normed[B32 * q:B32 * (q + 1), :, :]).then_inc(s_out, 16)

            for n, (name, row, panel, mine) in enumerate(chunks):
                last = n // PANELS - 1
                for u in mine:
                    hi(u)
                    for a in ended(u, AGG_AT, partials):
                        keep_partial(a)
                    if u == mine[0] and DIAGONALS <= last < GROUPS and n % PANELS == Y_AT:
                        make_y(last)
                    for a in ended(u, ELU_AT, rows_done):
                        if accs[a][2] == 0:
                            elu_parts(a)
                    for a in ended(u, MOMENTS_AT, rows_done):
                        moments(a)
                    for a in ended(u, NORM_AT, rows_done):
                        normalise(a)
                if not mine and DIAGONALS <= last < GROUPS and n % PANELS == Y_AT:
                    make_y(last)
                if name == "A":
                    raw_loaded(act, n)
                    deg_part(n)
                if 0 <= last < DIAGONALS and n % PANELS == 0:
                    make_y(last)
                if name == "A" and n % PANELS == (2 if row < DIAGONALS else 3):
                    keep_xt(row)
            for u in range(U, U + NORM_AT + 1):
                for a in ended(u, MOMENTS_AT, rows_done):
                    moments(a)
                for a in ended(u, NORM_AT, rows_done):
                    normalise(a)
            act.wait_ge(s_out, 16 * STRIPES * GROUPS)

        @block.vector
        def _(dve):
            def turn(u):
                name, row, col, n, _ = units[u]
                if u >= 2:
                    dve.wait_ge(s_hi, halves_of(u - 2, 1))
                    dve.wait_ge(s_lo, halves_of(u - 2, 1))
                own = accs[units[u][4]][2] == 0 and row == col
                src = raw[buffer_of[n]][:].rearrange("p b (t h c) -> p h t b c", h=2, c=B32)[:, col % 2]
                dst = turned[u % 2][:].rearrange("p t (b r) -> p t b r", r=B32)
                ins = nc.vector.transpose(dst, src)
                ins.then_inc(s_block if own else s_turn, 1)
                if own:
                    dve.wait_ge(s_block, row + 1)
                    for t in range(GT):
                        diag = turned[u % 2][:, t, :].rearrange("p (q t r) -> p t q r", q=STRIPES, r=B32)[:, t]
                        ins = nc.vector.tensor_tensor(diag, diag, ident[:].rearrange("p (q r) -> p q r", r=B32), ALU.add)
                    ins.then_inc(s_turn, 1)

            def lo(u):
                dve.wait_ge(s_turn, u + 1)
                for half, part in HALVES:
                    dve.wait_ge(s_hi, halves_of(u, half))
                    if u >= 2:
                        dve.wait_ge(s_used, halves_of(u - 2, half))
                    nc.vector.tensor_tensor(a_lo[u % 2][:, part, :], turned[u % 2][:, part, :],
                                            a_hi[u % 2][:, part, :].bitcast(F32),
                                            ALU.subtract).then_inc(s_lo, 1)

            def deg_part(n):
                _, row, panel, _ = chunks[n]
                mine = slice(0, DVE_BLOCKS[row])
                nc.vector.tensor_reduce(deg_parts[:, row % 2, panel, mine], raw[buffer_of[n]][:, mine, :], AX_X,
                                        ALU.add).then_inc(s_degd, 1)

            def deg_sum(row):
                dve.wait_ge(s_degd, PANELS * (row + 1))
                dve.wait_ge(s_dega, act_degs[row + 1])
                if row:
                    dve.wait_ge(s_dmm, row)
                nc.vector.tensor_reduce(deg_sums[:], deg_parts[:, row % 2, :, :].rearrange("p g b -> p b g"),
                                        AX_X, ALU.add).then_inc(s_dsum, 1)

            def deg_row(row):
                dve.wait_ge(s_dmm, row + 1)
                if row:
                    dve.wait_ge(s_pow, row)
                nc.vector.tensor_scalar(deg[:], acc[2][:, 0, 0:GT], 1.0, None, ALU.add).then_inc(s_deg, 1)

            def v_low(i, row):
                dve.wait_ge(s_vhi, i + 1)
                nc.vector.tensor_tensor(v_lo[:, tiles(row), :], normed[:], v_hi[:, tiles(row), :].bitcast(F32),
                                        ALU.subtract).then_inc(s_v, 1)

            def aggregate(a):
                i, row = order_of[a], accs[a][1]
                dve.wait_ge(s_used, halves_of(accs[a][4], 1))
                if i:
                    dve.wait_ge(s_proj, i)
                else:
                    dve.wait_ge(s_dega, act_degs[GROUPS])
                    dve.wait_ge(s_turn, units_through[THIRD])
                kept = next((partial_of[k] for k in partials if accs[k][1:3] == accs[a][1:3]), None)
                if kept is not None:
                    dve.wait_ge(s_part, kept + 1)
                for h in range(CH):
                    dst = agg[:, h, :].rearrange("p (t q r) -> p q t r", t=GT, q=STRIPES)
                    src = acc[bank_of[a]][:, h, :].rearrange("p (q t r) -> p q t r", t=GT, q=STRIPES)
                    if kept is not None:
                        ins = nc.vector.tensor_tensor(dst, src, partial[:, row, h, :].rearrange("p (q t r) -> p q t r", t=GT, q=STRIPES), ALU.add)
                    else:
                        ins = nc.vector.tensor_copy(dst, src)
                ins.then_inc(s_agg, 1)

            def residual(a):
                i, (_, row, layer, _, _) = order_of[a], accs[a]
                if layer == 0:
                    dve.wait_ge(s_elu, (GT + 1) * (i + 1))
                    dve.wait_ge(s_resx, i + 1)
                    nc.vector.scalar_tensor_tensor(out=res, in0=neg, scalar=-1.0, in1=res,
                                                   op0=ALU.add, op1=ALU.add).then_inc(s_res, 1)
                else:
                    dve.wait_ge(s_proj, i + 1)
                    dve.wait_ge(s_norm, GT * i)
                    nc.vector.tensor_tensor(res, proj[:], b_sb[:].rearrange("p (a n) -> p a n", a=1).to_broadcast([P, GT, C]),
                                            ALU.add).then_inc(s_res, 1)
                    dve.wait_ge(s_resx, i + 1)
                    dve.wait_ge(s_res, GROUPS + 2 * (i - GROUPS) + 1)
                    nc.vector.scalar_tensor_tensor(out=res, in0=res, scalar=0.0, in1=x_row[:],
                                                   op0=ALU.max, op1=ALU.add).then_inc(s_res, 1)

            def low_and_later(u):
                if lows_done[0] > u:
                    return
                lows_done[0] = u + 1
                lo(u)
                for a in ended(u, AGG_AT, rows_done):
                    aggregate(a)
                for a in ended(u, RESIDUAL_AT, rows_done):
                    residual(a)
                for a in ended(u, NORM_AT, rows_done):
                    if accs[a][2] == 0:
                        v_low(GROUPS + order_of[a], accs[a][1])

            lows_done = [0]

            dve.wait_ge(s_wt_mm, 1)
            nc.vector.tensor_copy(wt_sb[:].rearrange("p h n -> p (h n)"),
                                  proj[:, 0:CH, :].rearrange("p h n -> p (h n)")).then_inc(s_wt, 1)
            dve.wait_ge(s_const, 1)

            for n, (name, row, panel, mine) in enumerate(chunks):
                done, at = divmod(n, PANELS)
                last = done - 1
                if 0 <= last < GROUPS and at == (1 if last < DIAGONALS else 3):
                    v_low(last, last)
                raw_loaded(dve, n)
                for u in mine:
                    turn(u)
                    if u != mine[0] or name != "A":
                        low_and_later(u - 1)
                if name == "A":
                    deg_part(n)
                if DIAGONALS <= last < GROUPS and at == 0:
                    deg_row(last)
                if name == "A" and mine:
                    low_and_later(mine[-1])
                if at == PANELS - 1 and done < GROUPS:
                    deg_sum(done)
                if 0 <= last < DIAGONALS and at == 0:
                    deg_row(last)
            lo(U - 1)
            for u in range(U - 1, U + NORM_AT + 1):
                for a in ended(u, AGG_AT, rows_done):
                    aggregate(a)
                for a in ended(u, RESIDUAL_AT, rows_done):
                    residual(a)

        @block.tensor
        def _(pe):
            pe.wait_ge(s_const, 1)
            pe.wait_ge(s_w, 48)
            for h in range(CH):
                for g in range(CH):
                    ins = pe.transpose(proj[:, h, P * g:P * (g + 1)], normed[:, g, P * h:P * (h + 1)], ident[:])
            ins.then_inc(s_wt_mm, 1)
            pe.wait_ge(s_const, 1 + STRIPES)
            pe.wait_ge(s_wt, 1)

            def fold_degrees(row):
                pe.wait_ge(s_dsum, row + 1)
                if row:
                    pe.wait_ge(s_deg, row)
                for q in range(STRIPES):
                    ins = pe.matmul(acc[2][B32 * q:B32 * (q + 1), 0, 0:GT], fold[:], deg_sums[:, GT * q:GT * (q + 1)],
                                    start=True, stop=True)
                ins.then_inc(s_dmm, 1)

            def turn_x(row):
                pe.wait_ge(s_x, 64 * (row + 1))
                if row:
                    pe.wait_ge(s_yf, row)
                flat = proj[:].rearrange("p t n -> p (t n)")
                for h in range(CH):
                    for t in range(GT):
                        ins = pe.transpose(flat[:, GN * h + P * t:GN * h + P * (t + 1)], x_row[:, t, P * h:P * (h + 1)], ident[:])
                ins.then_inc(s_xt_mm, 1)

            def project_x(row):
                pe.wait_ge(s_xt, row + 1)
                flat = x_row[:].rearrange("p t n -> p (t n)")
                for t in range(GT):
                    for h in range(CH):
                        ins = pe.matmul(proj[:, t, :], flat[:, GN * h + P * t:GN * h + P * (t + 1)], w_sb[:, h, :],
                                        start=(h == 0), stop=(h == CH - 1))
                ins.then_inc(s_xw, 1)

            def project(a):
                i, layer = order_of[a], accs[a][2]
                pe.wait_ge(s_agg, i + 1)
                if i == 0:
                    pe.wait_ge(s_yf, GROUPS)
                elif i <= GROUPS:
                    pe.wait_ge(s_elu, (GT + 1) * i)
                else:
                    pe.wait_ge(s_res, GROUPS + 2 * (i - 1 - GROUPS) + 1)
                for t in range(GT):
                    for h in range(CH):
                        nodes = agg[:, h, P * t:P * (t + 1)]
                        if layer == 0:
                            ins = pe.transpose(proj[:, t, P * h:P * (h + 1)], nodes, ident[:])
                        else:
                            ins = pe.matmul(proj[:, t, :], nodes, wt_sb[:, h, :], start=(h == 0), stop=(h == CH - 1))
                ins.then_inc(s_proj, 1)

            def acc_free(a):
                old = acc_before[a]
                if old is None:
                    if bank_of[a] == 2:
                        pe.wait_ge(s_deg, GROUPS)
                elif old in order_of:
                    pe.wait_ge(s_agg, order_of[old] + 1)
                else:
                    pe.wait_ge(s_part, partial_of[old] + 1)

            def product(u):
                name, row, col, n, a = units[u]
                _, _, layer, first, last = accs[a]
                if u == first:
                    acc_free(a)
                pe.wait_ge(s_v, col + 1 if layer == 0 else GROUPS + col + 1)
                tile0 = tiles(col).start
                for t in range(GT):
                    if t % 2 == 0:
                        pe.wait_ge(s_hi, halves_of(u, t // 2))
                        pe.wait_ge(s_lo, halves_of(u, t // 2))
                    k = tile0 + 2 * t
                    for h in range(CH):
                        ch = slice(P * h, P * (h + 1))
                        dst = acc[bank_of[a]][:, h, :]
                        begin = u == first and t == 0
                        end = u == last and t == GT - 1
                        pe.matmul(dst, v_hi[:, k, ch], a_hi[u % 2][:, t, :], start=begin, stop=False)
                        pe.matmul(dst, v_hi[:, k, ch], a_lo[u % 2][:, t, :], start=False, stop=False)
                        ins = pe.matmul(dst, v_lo[:, k, ch], a_hi[u % 2][:, t, :], start=False, stop=end)
                    if t % 2:
                        ins.then_inc(s_used, 1)

            for n, (name, row, panel, mine) in enumerate(chunks):
                for u in mine:
                    if name == "A" and units[u][2] == row:
                        fold_degrees(row)
                        project_x(row)
                    elif name == "A" and row >= DIAGONALS and u == last_in_a[row]:
                        fold_degrees(row)
                    product(u)
                    for a in ended(u, PROJECT_AT, rows_done):
                        project(a)
                if name == "A" and n % PANELS == (1 if row < DIAGONALS else 2):
                    turn_x(row)
                if name == "A" and n % PANELS == PANELS - 1 and row >= DIAGONALS:
                    project_x(row)
            for u in range(U, U + PROJECT_AT + 1):
                for a in ended(u, PROJECT_AT, rows_done):
                    project(a)


_INS = ["x", "adj", "L0_gnn_w", "L1_gnn_W", "L1_gnn_b"]


def kernel(**inputs):
    import numpy as _np
    import concourse.bacc as _bacc
    from concourse import mybir as _mybir
    from concourse.bass_utils import run_bass_kernel_spmd as _run

    nc = _bacc.Bacc("TRN2", target_bir_lowering=False, num_devices=1)
    arrays, args = {}, []
    for name in _INS:
        a = _np.ascontiguousarray(inputs[name])
        arrays[f"in_{name}_dram"] = a
        args.append(nc.dram_tensor(f"in_{name}_dram", a.shape, _mybir.dt.from_np(a.dtype), kind="ExternalInput").ap())
    shape = tuple(inputs["x"].shape)
    args.append(nc.dram_tensor("out_0_dram", shape, _mybir.dt.float32, kind="ExternalOutput").ap())
    gnn_two_layers(nc, *args)
    r = _run(nc, [arrays], core_ids=[0])
    return r.results[0]["out_0_dram"]
```
